# Optimizing a Trainium2 kernel written in Bass

```python
import numpy as np
import jax
import jax.numpy as jnp

def _softmax(x, axis=-1):
    return jax.nn.softmax(x, axis=axis)

def _gelu(x):
    return jax.nn.gelu(x, approximate=True)

def _silu(x):
    return jax.nn.silu(x)

def _sigmoid(x):
    return jax.nn.sigmoid(x)

def _layernorm(x, axis=-1, eps=1e-05):
    m = jnp.mean(x, axis=axis, keepdims=True)
    v = jnp.var(x, axis=axis, keepdims=True)
    return (x - m) / jnp.sqrt(v + eps)

def _scatter_add(tgt, idx, src, axis=0):
    return tgt.at[idx].add(src)

def _segment_sum(src, seg, n):
    return jax.ops.segment_sum(src, seg, n)
kernel_name = 'mk_cond_resid_d2_seqx_r8_c2f0b0'

def setup_inputs(seed: int=0):
    np.random.seed(seed)
    _w = jnp.asarray

    def _rec_inputs():
        import jax
        import jax.numpy as jnp
        _rk = jax.random.key(seed)
        x = -0.000125 + 0.9999 * jax.random.normal(jax.random.fold_in(_rk, 1), (32, 128, 128), jnp.float32)
        _lenS = 128 - jax.random.randint(jax.random.fold_in(_rk, 7), (32,), 0, max(1, 128 // 4) + 1, jnp.int32)
        _lenS2 = 128 - jax.random.randint(jax.random.fold_in(_rk, 8), (32,), 0, max(1, 128 // 4) + 1, jnp.int32)
        cond_1024 = -0.00493535 + 1.00056 * jax.random.normal(jax.random.fold_in(_rk, 11), (32, 128), jnp.float32)
        return (x, cond_1024)
    x, cond_1024 = _rec_inputs()

    def _L0_cond_setup():
        import jax, jax.numpy as jnp
        import numpy as np
        import math
        N, T, D, H = (64, 64, 128, 128)
        key = jax.random.key(seed)
        k1, k2, k3, k4 = jax.random.split(key, 4)
        x = jax.random.normal(k1, (N, T, D), dtype=jnp.float32)
        h0 = jax.random.normal(k2, (N, H), dtype=jnp.float32)
        Wx = jax.random.normal(k3, (D, 4 * H), dtype=jnp.float32) / math.sqrt(D)
        Wh = jax.random.normal(k4, (H, 4 * H), dtype=jnp.float32) / math.sqrt(H)
        b = jnp.zeros((4 * H,), dtype=jnp.float32)
        return {'x': x, 'h0': h0, 'Wx': Wx, 'Wh': Wh, 'b': b}
    _L0_cond_all = _L0_cond_setup()
    _L0_cond_in = {k: v for k, v in _L0_cond_all.items() if k in ('Wx', 'Wh', 'b')}
    del _L0_cond_all

    def _L1_cond_setup():
        import jax, jax.numpy as jnp
        from jax import lax
        import numpy as np
        B, T, U = (64, 64, 128)
        key = jax.random.key(seed)
        k1, k2, k3 = jax.random.split(key, 3)
        x = jax.random.normal(k1, (B, T, U), dtype=jnp.float32)
        h0 = jax.random.normal(k2, (B, U), dtype=jnp.float32)
        limit = float(np.sqrt(6.0 / (2 * U + 2 * U)))
        weight = jax.random.uniform(k3, (2 * U, 2 * U), minval=-limit, maxval=limit, dtype=jnp.float32)
        bias = jnp.zeros((2 * U,), dtype=jnp.float32)
        return {'x': x, 'h0': h0, 'weight': weight, 'bias': bias}
    _L1_cond_all = _L1_cond_setup()
    _L1_cond_in = {k: v for k, v in _L1_cond_all.items() if k in ('weight', 'bias')}
    del _L1_cond_all
    return {'x': x, 'cond_1024': cond_1024, 'L0_cond_Wx': _L0_cond_in['Wx'], 'L0_cond_Wh': _L0_cond_in['Wh'], 'L0_cond_b': _L0_cond_in['b'], 'L1_cond_weight': _L1_cond_in['weight'], 'L1_cond_bias': _L1_cond_in['bias']}

def reference(x, cond_1024, L0_cond_Wx, L0_cond_Wh, L0_cond_b, L1_cond_weight, L1_cond_bias):
    import jax
    import jax.numpy as jnp

    def _L0_cond_ref(x, h0, Wx, Wh, b):
        import jax, jax.numpy as jnp
        import numpy as np
        import math
        N, T, D, H = (64, 64, 128, 128)
        Hdim = h0.shape[1]
        xW = jnp.einsum('ntd,dg->ntg', x, Wx) + b

        def step(carry, xw_t):
            prev_h, prev_c = carry
            a = xw_t + prev_h @ Wh
            i = jax.nn.sigmoid(a[:, :Hdim])
            f = jax.nn.sigmoid(a[:, Hdim:2 * Hdim])
            o = jax.nn.sigmoid(a[:, 2 * Hdim:3 * Hdim])
            g = jnp.tanh(a[:, 3 * Hdim:])
            next_c = f * prev_c + i * g
            next_h = o * jnp.tanh(next_c)
            return ((next_h, next_c), next_h)
        c0 = jnp.zeros_like(h0)
        _, hs = jax.lax.scan(step, (h0, c0), jnp.swapaxes(xW, 0, 1))
        return jnp.swapaxes(hs, 0, 1)

    def _L1_cond_ref(x, h0, weight, bias):
        import jax, jax.numpy as jnp
        from jax import lax
        import numpy as np
        B, T, U = (64, 64, 128)
        'UGRNN cell scanned over time. x:[B,T,U], h0:[B,U] -> outputs [B,T,U].'
        units = h0.shape[-1]

        def step(h, xt):
            cell_inputs = jnp.concatenate([xt, h], axis=-1)
            m = cell_inputs @ weight + bias
            g_act = m[:, :units]
            c_act = m[:, units:]
            c = jnp.tanh(c_act)
            g = jax.nn.sigmoid(g_act + 1.0)
            h_new = g * h + (1.0 - g) * c
            return (h_new, h_new)
        xs = jnp.swapaxes(x, 0, 1)
        _, ys = lax.scan(step, h0, xs)
        return jnp.swapaxes(ys, 0, 1)
    x = x + _L0_cond_ref(x, cond_1024, L0_cond_Wx, L0_cond_Wh, L0_cond_b)
    x = x + _L1_cond_ref(x, cond_1024, L1_cond_weight, L1_cond_bias)
    return x

_drawn_inputs = setup_inputs


def setup_inputs(seed=0):
    import zlib

    import numpy as np

    out = dict(_drawn_inputs(seed))
    spreads = {'L0_cond_b': (0.0, 0.1), 'L1_cond_bias': (0.0, 0.1)}
    factors = {}
    for name, (base, spread) in spreads.items():
        noise = np.random.default_rng([zlib.crc32(name.encode()), seed]).standard_normal(out[name].shape)
        drawn = base * np.exp(spread * noise) if base else spread * noise
        out[name] = jnp.asarray(drawn.astype(out[name].dtype))
    for name, factor in factors.items():
        out[name] = (out[name] * factor).astype(out[name].dtype)
    return out
```

```python
import concourse.bass as bass
from concourse import mybir
from contextlib import ExitStack

F32 = mybir.dt.float32
BF16 = mybir.dt.bfloat16
ALU = mybir.AluOpType
ACT = mybir.ActivationFunctionType

P = 128
N = 32
T = 128
GS = 4
GROUPS = T // GS
BODY = 2 * GS
LAG = GS

GATES = ("o", "i", "f", "g")
SOURCE = {"i": 0, "f": 1, "o": 2, "g": 3}
NG = len(GATES)


def two_layer_recurrence(nc, x, h_first, wx, wh, b0, w1, b1, out):
    x_g = x.rearrange("n (g t) d -> g t n d", t=GS)
    out_g = out.rearrange("n (g t) d -> g t n d", t=GS)
    ctx = ExitStack()
    with ctx:
        def sb(name, shape, dt=F32):
            return ctx.enter_context(nc.sbuf_tensor(name, shape, dt))

        def bank(name):
            return ctx.enter_context(nc.psum_tensor(name, [P, 512], F32))

        def sem(name):
            return ctx.enter_context(nc.semaphore(name))

        x_rows = sb("x_rows", [P, 2, P])
        cond_rows = sb("cond_rows", [N, P])
        wx_raw = sb("wx_raw", [P, NG * P])
        wh_raw = sb("wh_raw", [P, NG * P])
        w1_raw = sb("w1_raw", [P, 2, 2 * P])
        bias_rows = sb("bias_rows", [P, P])
        wx_s = sb("wx_s", [P, NG, P])
        wh_s = sb("wh_s", [P, NG, P])
        w1_s = sb("w1_s", [P, 2, 2, P])
        rest_mid = sb("rest_mid", [P, P])
        rest_low = sb("rest_low", [P, P])
        part = sb("part", [P, 3, P], BF16)
        bias_lhs = sb("bias_lhs", [P, P], BF16)
        pick_sum = sb("pick_sum", [P, 6])
        pick = sb("pick", [P, 6], BF16)
        ident = sb("ident", [P, P])
        xT = sb("xT", [P, 2, GS, N])
        x1T = sb("x1T", [P, 2, GS, N])
        hT = sb("hT", [P, BODY, N])
        uT = sb("uT", [P, BODY, N])
        sumT = sb("sumT", [P, GS, N])
        acts = sb("acts", [P, 2, (NG + 1) * N])
        pair = sb("pair", [P, 2 * N])
        tanh_c = sb("tanh_c", [P, 2, N])
        acts1 = sb("acts1", [P, 2, 2 * N])
        diff = sb("diff", [P, N])
        gated = sb("gated", [P, N])
        out_rows = sb("out_rows", [P, 2, P])

        a0 = [bank(f"a0_{i}") for i in range(2)]
        ao = [bank(f"ao_{i}") for i in range(2)]
        a1 = [bank(f"a1_{i}") for i in range(2)]
        xT_ps = bank("xT_ps")
        out_ps = bank("out_ps")

        x_in = [sem(f"x_in{i}") for i in range(2)]
        cond_in = sem("cond_in")
        wx_in, wh_in, w1_in, b_in = sem("wx_in"), sem("wh_in"), sem("w1_in"), sem("b_in")
        out_stored = [sem(f"out_stored{i}") for i in range(2)]
        ident_zero, ident_ready = sem("ident_zero"), sem("ident_ready")
        rows_zero = sem("rows_zero")
        wx_ready, wh_ready, w1_ready = sem("wx_ready"), sem("wh_ready"), sem("w1_ready")
        bias_step, bias_ready = sem("bias_step"), sem("bias_ready")
        cond_turned = sem("cond_turned")
        ifg_summed, o_summed = sem("ifg_summed"), sem("o_summed")
        ifg_ready, o_ready = sem("ifg_ready"), sem("o_ready")
        pair_ready, cell_ready, tanh_c_ready = sem("pair_ready"), sem("cell_ready"), sem("tanh_c_ready")
        h_ready = sem("h_ready")
        a1_summed, acts1_ready = sem("a1_summed"), sem("acts1_ready")
        diff_ready, gated_ready = sem("diff_ready"), sem("gated_ready")
        u_ready = sem("u_ready")
        x_turned, xT_ready, x1_ready = sem("x_turned"), sem("xT_ready"), sem("x1_ready")
        sum_ready, out_turned, out_ready = sem("sum_ready"), sem("out_turned"), sem("out_ready")

        block = ctx.enter_context(nc.Block())

        def a0_group(c):
            return a0[c][:, 0:GS * 3 * N].rearrange("p (t g n) -> p t g n", t=GS, g=3)

        def ao_group(c):
            return ao[c][:, 0:GS * N].rearrange("p (t n) -> p t n", t=GS)

        def a0_step(j):
            o = (j % GS) * 3 * N
            return a0[j // GS % 2][:, o:o + 3 * N]

        def ao_step(j):
            o = (j % GS) * N
            return ao[j // GS % 2][:, o:o + N]

        def a1_step(j):
            o = (j % GS) * 2 * N
            return a1[j // GS % 2][:, o:o + 2 * N]

        def schedule(eng, body):
            body(0, True, False)
            with eng.Fori(BODY, T - BODY, BODY) as s0:
                body(s0, False, False)
            body(T - BODY, False, True)

        @block.gpsimd
        def _(pool):
            nc.gpsimd.memset(bias_rows[:, :], 0.0).then_inc(ident_zero, 1)
            nc.gpsimd.memset(ident[:, :], 0.0).then_inc(ident_zero, 1)
            pool.wait_ge(ident_zero, 2)
            nc.gpsimd.affine_select(out=ident[:, :], in_=ident[:, :], compare_op=ALU.not_equal, fill=1.0,
                                    base=0, pattern=[[-1, P]], channel_multiplier=1).then_inc(ident_ready, 1)
            nc.gpsimd.affine_select(out=bias_rows[:, :], in_=bias_rows[:, :], compare_op=ALU.not_equal,
                                    fill=1.0, base=-6, pattern=[[0, P]],
                                    channel_multiplier=1).then_inc(rows_zero, 1)

        @block.sync
        def _(sp):
            def load_x(g, slot):
                for t in range(GS):
                    sp.dma_start(x_rows[t * N:(t + 1) * N, slot, :], x_g[g, t]).then_inc(x_in[slot], 16)

            def store_out(g, slot):
                for t in range(GS):
                    sp.dma_start(out_g[g, t], out_rows[t * N:(t + 1) * N, slot, :]).then_inc(out_stored[slot], 16)

            load_x(0, 0)
            sp.dma_start(wx_raw[:, :], wx).then_inc(wx_in, 16)
            sp.dma_start(w1_raw[:, :, :], w1.rearrange("(h k) n -> k h n", h=2)).then_inc(w1_in, 16)
            load_x(1, 1)
            sp.wait_ge(x_turned, GS)
            load_x(2, 0)

            def body(s0, first, last):
                g0 = s0 // GS if isinstance(s0, int) else s0 // GS
                for c in range(2):
                    s = s0 + c * GS
                    if not (last):
                        sp.wait_ge(x_turned, s + 2 * GS)
                        load_x(g0 + c + 3, (c + 1) % 2) if not (last) else None
                    if not first:
                        sp.wait_ge(out_ready, s - GS)
                        store_out(g0 + c - 2, c)

            body(0, True, False)
            with sp.Fori(BODY, T - 2 * BODY, BODY) as s0:
                body(s0, False, False)
            for s in range(T - 2 * BODY, T, GS):
                g = s // GS
                if g + 3 < GROUPS:
                    sp.wait_ge(x_turned, s + 2 * GS)
                    load_x(g + 3, (g + 1) % 2)
                sp.wait_ge(out_ready, s - GS)
                store_out(g - 2, g % 2)
            for g in range(GROUPS, GROUPS + 2):
                sp.wait_ge(out_ready, GS * (g - 1))
                store_out(g - 2, g % 2)
            for c in range(2):
                sp.wait_ge(out_stored[c], 16 * GS * GROUPS // 2)

        @block.tensor
        def _(pe):
            def turn_x(slot):
                nc.tensor.transpose(xT_ps[:, 0:P], x_rows[:, slot, :], ident[:, :]).then_inc(x_turned, GS)

            def bias0(c):
                nc.tensor.matmul(a0_group(c), bias_lhs[:, :],
                                 pick[:, 1:NG].unsqueeze(1).unsqueeze(3).to_broadcast([P, GS, 3, N]),
                                 start=True, stop=False, skip_group_check=True)
                nc.tensor.matmul(ao_group(c), bias_lhs[:, :],
                                 pick[:, 0:1].unsqueeze(1).to_broadcast([P, GS, N]),
                                 start=True, stop=False, skip_group_check=True)

            def project0(c, q):
                nc.tensor.matmul(a0_group(c)[:, :, q - 1, :] if q else ao_group(c),
                                 wx_s[:, q, :], xT[:, c, :, :], start=False, stop=False, skip_group_check=True)

            def bias1(c):
                nc.tensor.matmul(a1[c][:, 0:GS * 2 * N].rearrange("p (t g n) -> p t g n", t=GS, g=2),
                                 bias_lhs[:, :],
                                 pick[:, NG:NG + 2].unsqueeze(1).unsqueeze(3).to_broadcast([P, GS, 2, N]),
                                 start=True, stop=False, skip_group_check=True)

            def project1(c, q):
                nc.tensor.matmul(a1[c][:, 0:GS * 2 * N].rearrange("p (t g n) -> p t g n", t=GS, g=2)[:, :, q, :],
                                 w1_s[:, 0, q, :], x1T[:, c, :, :], start=False, stop=False,
                                 skip_group_check=True)

            def layer0(s, j):
                pe.wait_ge(h_ready, s + 1)
                for q in (1, 2, 3, 0):
                    mm = nc.tensor.matmul(a0_step(j)[:, (q - 1) * N:q * N] if q else ao_step(j), wh_s[:, q, :],
                                          hT[:, (j - 1) % BODY, :], start=False, stop=True,
                                          skip_group_check=True)
                    if q == 3:
                        mm.then_inc(ifg_summed, 1)
                mm.then_inc(o_summed, 1)

            def layer1(r, j):
                pe.wait_ge(u_ready, r + 1)
                for q in range(2):
                    mm = nc.tensor.matmul(a1_step(j)[:, q * N:(q + 1) * N], w1_s[:, 1, q, :],
                                          uT[:, (j - 1) % BODY, :], start=False, stop=True,
                                          skip_group_check=True)
                mm.then_inc(a1_summed, 1)

            def start_layer1_group(r, c):
                pe.wait_ge(x1_ready, r + GS)
                bias1(c)
                project1(c, 0)
                project1(c, 1)

            pe.wait_ge(ident_ready, 1)
            pe.wait_ge(cond_in, 16)
            nc.tensor.transpose(out_ps[:, 0:N], cond_rows[:, :], ident[0:N, 0:N]).then_inc(cond_turned, 1)
            pe.wait_ge(x_in[0], 16 * GS)
            turn_x(0)
            pe.wait_ge(bias_ready, 1)
            bias0(0)
            pe.wait_ge(wx_ready, 1)
            pe.wait_ge(xT_ready, GS)
            for q in range(NG):
                project0(0, q)
            pe.wait_ge(wh_ready, 1)

            def body(s0, first, last):
                for j in range(BODY):
                    s, c, k = s0 + j, j // GS, j % GS
                    other = (c + 1) % 2
                    more = not (last and c == 1)
                    layer0(s, j)
                    if k == 0 and more:
                        pe.wait_ge(x_in[other], 16 * GS // BODY * (s0 + (1 if c else 0) * BODY + BODY) if c else
                                   16 * GS // BODY * (s0 + BODY))
                        turn_x(other)
                    if k == 0 and not (first and c == 0):
                        if first:
                            pe.wait_ge(w1_ready, 1)
                        start_layer1_group(s - LAG, other)
                    if not (first and c == 0):
                        layer1(s - LAG, (j - LAG) % BODY)
                    if k == 1 and more:
                        bias0(other)
                        pe.wait_ge(xT_ready, s - 1 + 2 * GS)
                        project0(other, 0)
                        project0(other, 1)
                    if k == 2:
                        if not first:
                            pe.wait_ge(sum_ready, s - 2 - GS)
                            nc.tensor.transpose(out_ps[:, 0:P], sumT[:, :, :].rearrange("p t n -> p (t n)"),
                                                ident[:, :]).then_inc(out_turned, GS)
                        if more:
                            project0(other, 2)
                    if k == 3 and more:
                        project0(other, 3)

            schedule(pe, body)
            start_layer1_group(T - LAG, 1)
            for k in range(GS):
                layer1(T - LAG + k, GS + k)
            for g in range(GROUPS, GROUPS + 2):
                pe.wait_ge(sum_ready, GS * (g - 1))
                if g > GROUPS:
                    pe.wait_ge(out_ready, GS * (g - 2))
                nc.tensor.transpose(out_ps[:, 0:P], sumT[:, :, :].rearrange("p t n -> p (t n)"),
                                    ident[:, :]).then_inc(out_turned, GS)

        @block.scalar
        def _(act):
            def copy_xT(c, count):
                act.wait_ge(x_turned, count)
                nc.scalar.activation(xT[:, c, :, :].rearrange("p t n -> p (t n)"), xT_ps[:, 0:P],
                                     ACT.Copy).then_inc(xT_ready, GS)

            def copy_out(c, count, stored):
                act.wait_ge(out_turned, count)
                if stored is not None:
                    act.wait_ge(out_stored[c], stored)
                nc.scalar.activation(out_rows[:, c, :], out_ps[:, 0:P], ACT.Copy).then_inc(out_ready, GS)

            def layer0(s, j):
                act.wait_ge(ifg_summed, s + 1)
                nc.scalar.activation(acts[:, j % 2, N:NG * N], a0_step(j),
                                     ACT.Tanh).then_inc(ifg_ready, 1)
                act.wait_ge(o_summed, s + 1)
                nc.scalar.activation(acts[:, j % 2, 0:N], ao_step(j), ACT.Tanh).then_inc(o_ready, 1)
                act.wait_ge(cell_ready, s + 1)
                nc.scalar.activation(tanh_c[:, j % 2, :], acts[:, (j + 1) % 2, NG * N:(NG + 1) * N], ACT.Tanh,
                                     scale=0.5).then_inc(tanh_c_ready, 1)

            def layer1(r, j):
                act.wait_ge(a1_summed, r + 1)
                nc.scalar.activation(acts1[:, j % 2, :], a1_step(j), ACT.Tanh).then_inc(acts1_ready, 1)

            act.dma_start(cond_rows[:, :], h_first).then_inc(cond_in, 16)
            act.dma_start(wh_raw[:, :], wh).then_inc(wh_in, 16)
            act.wait_ge(rows_zero, 1)
            b0_v = b0.rearrange("(g n) -> g n", n=P)
            b1_v = b1.rearrange("(g n) -> g n", n=P)
            for q in range(3):
                r = 32 * q
                act.dma_start(bias_rows[r:r + 1, :], b0_v[2:3, :]).then_inc(b_in, 16)
                act.dma_start(bias_rows[r + 1:r + 3, :], b0_v[0:2, :]).then_inc(b_in, 16)
                act.dma_start(bias_rows[r + 3:r + 4, :], b0_v[3:4, :]).then_inc(b_in, 16)
                act.dma_start(bias_rows[r + 4:r + 6, :], b1_v[:, :]).then_inc(b_in, 16)
            copy_xT(0, GS)

            def body(s0, first, last):
                for j in range(BODY):
                    s, c, k = s0 + j, j // GS, j % GS
                    layer0(s, j)
                    if not (first and c == 0):
                        layer1(s - LAG, (j - LAG) % BODY)
                    if k == 0 and not (last and c == 1):
                        copy_xT((c + 1) % 2, s + 2 * GS)
                    if k == 3 and not first:
                        copy_out(c, s - 3 - GS, 16 * GS // BODY * (s0 - BODY))

            body(0, True, False)
            body1 = lambda: None
            for j in range(BODY):
                s, c, k = BODY + j, j // GS, j % GS
                layer0(s, j)
                layer1(s - LAG, (j - LAG) % BODY)
                if k == 0:
                    copy_xT((c + 1) % 2, s + 2 * GS)
                if k == 3:
                    copy_out(c, s - 3 - GS, None)
            with act.Fori(2 * BODY, T - BODY, BODY) as s0:
                body(s0, False, False)
            body(T - BODY, False, True)
            for k in range(GS):
                layer1(T - LAG + k, GS + k)
            for g in range(GROUPS, GROUPS + 2):
                copy_out(g % 2, GS * (g - 1), 16 * GS * (g // 2 - 1))

        @block.vector
        def _(dve):
            steps = [0]

            def then(ins):
                steps[0] += 1
                ins.then_inc(bias_step, 1)
                dve.wait_ge(bias_step, steps[0])

            def layer0(s, j):
                b, nxt = j % 2, (j + 1) % 2
                dve.wait_ge(ifg_ready, s + 1)
                nc.vector.scalar_tensor_tensor(out=pair[:, :], in0=acts[:, b, N:3 * N], scalar=1.0,
                                               in1=acts[:, b, 3 * N:5 * N], op0=ALU.add,
                                               op1=ALU.mult).then_inc(pair_ready, 1)
                dve.wait_ge(pair_ready, s + 1)
                nc.vector.scalar_tensor_tensor(out=acts[:, nxt, NG * N:(NG + 1) * N], in0=pair[:, N:2 * N],
                                               scalar=0.5, in1=pair[:, 0:N], op0=ALU.mult,
                                               op1=ALU.add).then_inc(cell_ready, 1)
                dve.wait_ge(o_ready, s + 1)
                dve.wait_ge(tanh_c_ready, s + 1)
                nc.vector.scalar_tensor_tensor(out=hT[:, j, :], in0=acts[:, b, 0:N], scalar=1.0,
                                               in1=tanh_c[:, b, :], op0=ALU.add,
                                               op1=ALU.mult).then_inc(h_ready, 1)

            def layer1(r, j):
                b = j % 2
                dve.wait_ge(acts1_ready, r + 1)
                nc.vector.tensor_tensor(diff[:, :], uT[:, (j - 1) % BODY, :], acts1[:, b, N:2 * N],
                                        ALU.subtract).then_inc(diff_ready, 1)
                dve.wait_ge(diff_ready, r + 1)
                nc.vector.scalar_tensor_tensor(out=gated[:, :], in0=acts1[:, b, 0:N], scalar=1.0,
                                               in1=diff[:, :], op0=ALU.add, op1=ALU.mult).then_inc(gated_ready, 1)
                dve.wait_ge(gated_ready, r + 1)
                nc.vector.scalar_tensor_tensor(out=uT[:, j, :], in0=gated[:, :], scalar=0.5,
                                               in1=acts1[:, b, N:2 * N], op0=ALU.mult,
                                               op1=ALU.add).then_inc(u_ready, 1)

            def add_layer0(c, count):
                dve.wait_ge(h_ready, count + 1)
                nc.vector.scalar_tensor_tensor(out=x1T[:, c, :, :].rearrange("p t n -> p (t n)"),
                                               in0=hT[:, c * GS:(c + 1) * GS, :].rearrange("p t n -> p (t n)"),
                                               scalar=0.5, in1=xT[:, c, :, :].rearrange("p t n -> p (t n)"),
                                               op0=ALU.mult, op1=ALU.add).then_inc(x1_ready, GS)

            def add_layer1(c, count):
                dve.wait_ge(u_ready, count + 1)
                nc.vector.tensor_tensor(sumT[:, :, :].rearrange("p t n -> p (t n)"),
                                        uT[:, c * GS:(c + 1) * GS, :].rearrange("p t n -> p (t n)"),
                                        x1T[:, c, :, :].rearrange("p t n -> p (t n)"),
                                        ALU.add).then_inc(sum_ready, GS)

            nc.vector.memset(acts[:, 0, NG * N:(NG + 1) * N], 0.0)
            dve.wait_ge(rows_zero, 1)
            dve.wait_ge(b_in, 16 * 12)
            then(nc.vector.tensor_copy(part[:, 0, :], bias_rows[:, :]))
            then(nc.vector.tensor_tensor(rest_mid[:, :], bias_rows[:, :], part[:, 0, :], ALU.subtract))
            then(nc.vector.tensor_copy(part[:, 1, :], rest_mid[:, :]))
            then(nc.vector.tensor_tensor(rest_low[:, :], rest_mid[:, :], part[:, 1, :], ALU.subtract))
            then(nc.vector.tensor_copy(part[:, 2, :], rest_low[:, :]))
            then(nc.vector.memset(bias_lhs[:, :], 0.0))
            for q in range(3):
                r = 32 * q
                then(nc.vector.tensor_copy(bias_lhs[r:r + 32, :], part[r:r + 32, q, :]))
            dve.wait_ge(ident_ready, 1)
            then(nc.vector.tensor_tensor(pick_sum[:, :], ident[:, 0:6], ident[:, 32:38], ALU.add))
            then(nc.vector.tensor_tensor(pick_sum[:, :], pick_sum[:, :], ident[:, 64:70], ALU.add))
            then(nc.vector.tensor_tensor(pick_sum[:, 4:5], pick_sum[:, 4:5], ident[:, 6:7], ALU.add))
            then(nc.vector.tensor_copy(pick[:, :], pick_sum[:, :]))
            then(nc.vector.tensor_scalar(pick[:, 0:3], pick_sum[:, 0:3], 0.5, None, ALU.mult))
            nc.vector.tensor_scalar(pick[:, 4:5], pick_sum[:, 4:5], 0.5, None, ALU.mult).then_inc(bias_ready, 1)
            dve.wait_ge(cond_turned, 1)
            nc.vector.tensor_scalar(hT[:, BODY - 1, :], out_ps[:, 0:N], 2.0, None, ALU.mult).then_inc(h_ready, 1)
            nc.vector.tensor_copy(uT[:, BODY - 1, :], out_ps[:, 0:N]).then_inc(u_ready, 1)
            dve.wait_ge(wx_in, 16)
            for q, name in enumerate(GATES):
                src = SOURCE[name] * P
                ins = nc.vector.tensor_scalar(wx_s[:, q, :], wx_raw[:, src:src + P],
                                              1.0 if name == "g" else 0.5, None, ALU.mult)
            ins.then_inc(wx_ready, 1)
            dve.wait_ge(wh_in, 16)
            for q, name in enumerate(GATES):
                src = SOURCE[name] * P
                ins = nc.vector.tensor_scalar(wh_s[:, q, :], wh_raw[:, src:src + P],
                                              0.5 if name == "g" else 0.25, None, ALU.mult)
            ins.then_inc(wh_ready, 1)
            dve.wait_ge(w1_in, 16)
            nc.vector.tensor_scalar(w1_s[:, :, 0, :], w1_raw[:, :, 0:P], 0.5, None, ALU.mult)
            nc.vector.tensor_copy(w1_s[:, :, 1, :], w1_raw[:, :, P:2 * P]).then_inc(w1_ready, 1)

            def body(s0, first, last):
                for j in range(BODY):
                    s, c, k = s0 + j, j // GS, j % GS
                    layer0(s, j)
                    if not (first and c == 0):
                        layer1(s - LAG, (j - LAG) % BODY)
                    if k == 0 and not first:
                        add_layer1(c, s - GS)
                    if k == 3:
                        dve.wait_ge(xT_ready, s + 1)
                        add_layer0(c, s + 1)

            schedule(dve, body)
            for k in range(GS):
                layer1(T - LAG + k, GS + k)
                if k == 0:
                    add_layer1(0, T - GS)
            dve.wait_ge(out_turned, T - GS)
            add_layer1(1, T)


_INS = ["x", "cond_1024", "L0_cond_Wx", "L0_cond_Wh", "L0_cond_b", "L1_cond_weight", "L1_cond_bias"]


def kernel(**inputs):
    import numpy as _np
    import concourse.bacc as _bacc
    from concourse import mybir as _mybir
    from concourse.bass_utils import run_bass_kernel_spmd as _run

    nc = _bacc.Bacc("TRN2", target_bir_lowering=False, num_devices=1)
    arrays, args = {}, []
    for name in _INS:
        a = _np.ascontiguousarray(inputs[name])
        arrays[f"in_{name}_dram"] = a
        args.append(nc.dram_tensor(f"in_{name}_dram", a.shape, _mybir.dt.from_np(a.dtype), kind="ExternalInput").ap())
    shape = inputs["x"].shape
    out = nc.dram_tensor("out_0_dram", shape, F32, kind="ExternalOutput").ap()
    two_layer_recurrence(nc, *args, out)
    r = _run(nc, [arrays], core_ids=[0])
    return r.results[0]["out_0_dram"]
```

```python
import concourse.bass as bass
from concourse import mybir
from contextlib import ExitStack

F32 = mybir.dt.float32
BF16 = mybir.dt.bfloat16
ALU = mybir.AluOpType
ACT = mybir.ActivationFunctionType

P = 128
N = 32
T = 128
GS = 4
GROUPS = T // GS
BODY = 2 * GS
QUADRANT = 32
SPLIT_STAGES = 4
ONE_ROW = 2 * QUADRANT + 6
LAG = GS

GATE_I, GATE_F, GATE_O, GATE_G = range(4)
NG = 4
IFG = (GATE_I, GATE_F, GATE_G)
SIGMOIDS = 3


def two_layer_recurrence(nc, x, h_first, wx, wh, b0, w1, b1, out):
    x_g = x.rearrange("n (g t) d -> g t n d", t=GS)
    out_g = out.rearrange("n (g t) d -> g t n d", t=GS)
    ctx = ExitStack()
    with ctx:
        def sb(name, shape, dt=F32):
            return ctx.enter_context(nc.sbuf_tensor(name, shape, dt))

        def bank(name):
            return ctx.enter_context(nc.psum_tensor(name, [P, 512], F32))

        def sem(name):
            return ctx.enter_context(nc.semaphore(name))

        x_rows = sb("x_rows", [P, 2, P])
        cond_rows = sb("cond_rows", [N, P])
        wx_raw = sb("wx_raw", [P, NG * P])
        wh_raw = sb("wh_raw", [P, NG * P])
        w1_raw = sb("w1_raw", [P, 2, 2 * P])
        bias_rows = sb("bias_rows", [P, P])
        wx_s = sb("wx_s", [P, NG, P])
        w1x_s = sb("w1x_s", [P, 2, P])
        wh_rest = sb("wh_rest", [P, NG * P])
        wh_part = sb("wh_part", [P, 3, NG * P], BF16)
        w1h_rest = sb("w1h_rest", [P, 2 * P])
        w1h_part = sb("w1h_part", [P, 3, 2 * P], BF16)
        bias_rest = sb("bias_rest", [P, P])
        bias_lhs = sb("bias_lhs", [P, P], BF16)
        pick_sum = sb("pick_sum", [P, NG + 2])
        pick = sb("pick", [P, NG + 2], BF16)
        ident = sb("ident", [P, P])
        xT = sb("xT", [P, 2, GS, N])
        x1T = sb("x1T", [P, 2, GS, N])
        hT = sb("hT", [P, BODY, N])
        h_rest = sb("h_rest", [P, 2, N])
        h_low = sb("h_low", [P, 2, N], BF16)
        sumT = sb("sumT", [P, GS, N])
        acts = sb("acts", [P, 2, (NG + 1) * N])
        acts_blank = sb("acts_blank", [P, 1])
        pair = sb("pair", [P, 2 * N])
        tanh_c = sb("tanh_c", [P, 2, N])
        acts1 = sb("acts1", [P, BODY, 4, N])
        pair1 = sb("pair1", [P, 2, N])
        u_rest = sb("u_rest", [P, 2, N])
        u_low = sb("u_low", [P, 2, N], BF16)
        out_rows = sb("out_rows", [P, 2, P])

        a0 = [bank(f"a0_{i}") for i in range(2)]
        ao = [bank(f"ao_{i}") for i in range(2)]
        a1 = [bank(f"a1_{i}") for i in range(2)]
        turned_ps = bank("turned_ps")
        xT_ps, out_ps = turned_ps[:, 0:P], turned_ps[:, P:2 * P]
        cell_ps = bank("cell_ps")

        x_in = [sem(f"x_in{i}") for i in range(2)]
        cond_in = sem("cond_in")
        wx_in, wh_in, w1_in, b_in = sem("wx_in"), sem("wh_in"), sem("w1_in"), sem("b_in")
        out_stored = [sem(f"out_stored{i}") for i in range(2)]
        ident_zero, ident_ready = sem("ident_zero"), sem("ident_ready")
        rows_zero = sem("rows_zero")
        wx_ready = sem("wx_ready")
        weights_split = sem("weights_split")
        bias_step, bias_ready = sem("bias_step"), sem("bias_ready")
        cond_turned = sem("cond_turned")
        ifg_summed, o_summed = sem("ifg_summed"), sem("o_summed")
        ifg_ready, o_ready = sem("ifg_ready"), sem("o_ready")
        pair_ready, cell_ready, tanh_c_ready = sem("pair_ready"), sem("cell_ready"), sem("tanh_c_ready")
        h_ready = sem("h_ready")
        a1_summed, acts1_ready = sem("a1_summed"), sem("acts1_ready")
        h_rest_ready, h_low_ready = sem("h_rest_ready"), sem("h_low_ready")
        pair1_ready = sem("pair1_ready")
        u_ready, u_rest_ready, u_low_ready = sem("u_ready"), sem("u_rest_ready"), sem("u_low_ready")
        blank_ready = sem("blank_ready")
        x_turned, xT_ready, x1_ready = sem("x_turned"), sem("xT_ready"), sem("x1_ready")
        sum_ready, out_turned, out_ready = sem("sum_ready"), sem("out_turned"), sem("out_ready")

        block = ctx.enter_context(nc.Block())

        def upper(ap):
            return ap.bitcast(BF16).rearrange("p (n two) -> p n two", two=2)[:, :, 1]

        def u_of(j):
            return acts1[:, (j + 1) % BODY, 2, :]

        def a0_group(c):
            return a0[c][:, 0:GS * 3 * N].rearrange("p (t g n) -> p t g n", t=GS, g=3)

        def ao_group(c):
            return ao[c][:, 0:GS * N].rearrange("p (t n) -> p t n", t=GS)

        def a0_step(j):
            o = (j % GS) * 3 * N
            return a0[j // GS % 2][:, o:o + 3 * N]

        def ao_step(j):
            o = (j % GS) * N
            return ao[j // GS % 2][:, o:o + N]

        def a1_step(j):
            o = (j % GS) * 2 * N
            return a1[j // GS % 2][:, o:o + 2 * N]

        def schedule(eng, body):
            body(0, True, False)
            with eng.Fori(BODY, T - BODY, BODY) as s0:
                body(s0, False, False)
            body(T - BODY, False, True)

        @block.gpsimd
        def _(pool):
            nc.gpsimd.memset(ident[:, :], 0.0).then_inc(ident_zero, 1)
            nc.gpsimd.memset(bias_rows[:, :], 0.0).then_inc(ident_zero, 1)
            pool.wait_ge(ident_zero, 2)
            nc.gpsimd.affine_select(out=bias_rows[:, :], in_=bias_rows[:, :], compare_op=ALU.not_equal,
                                    fill=1.0, base=-ONE_ROW, pattern=[[0, P]],
                                    channel_multiplier=1).then_inc(rows_zero, 1)
            nc.gpsimd.affine_select(out=ident[:, :], in_=ident[:, :], compare_op=ALU.not_equal, fill=1.0,
                                    base=0, pattern=[[-1, P]], channel_multiplier=1).then_inc(ident_ready, 1)
            pool.wait_ge(rows_zero, 1)
            for q in range(3):
                r = QUADRANT * q
                pool.dma_start(bias_rows[r:r + NG, :], b0.rearrange("(g n) -> g n", n=P)).then_inc(b_in, 16)
                pool.dma_start(bias_rows[r + NG:r + NG + 2, :],
                               b1.rearrange("(g n) -> g n", n=P)).then_inc(b_in, 16)

        @block.sync
        def _(sp):
            def load_x(g, slot):
                sp.dma_start(x_rows[:, slot, :], x_g[g]).then_inc(x_in[slot], 16)

            def store_out(g, slot):
                sp.dma_start(out_g[g], out_rows[:, slot, :]).then_inc(out_stored[slot], 16)

            load_x(0, 0)
            sp.dma_start(wx_raw[:, :], wx).then_inc(wx_in, 16)
            load_x(1, 1)
            sp.dma_start(w1_raw[:, :, :], w1.rearrange("(h k) n -> k h n", h=2)).then_inc(w1_in, 16)
            sp.wait_ge(x_turned, GS)
            load_x(2, 0)

            def body(s0, first, last):
                g0 = s0 // GS if isinstance(s0, int) else s0 // GS
                for c in range(2):
                    s = s0 + c * GS
                    if not (last):
                        sp.wait_ge(x_turned, s + 2 * GS)
                        load_x(g0 + c + 3, (c + 1) % 2) if not (last) else None
                    if not first:
                        sp.wait_ge(out_ready, s - GS)
                        store_out(g0 + c - 2, c)

            body(0, True, False)
            with sp.Fori(BODY, T - 2 * BODY, BODY) as s0:
                body(s0, False, False)
            for s in range(T - 2 * BODY, T, GS):
                g = s // GS
                if g + 3 < GROUPS:
                    sp.wait_ge(x_turned, s + 2 * GS)
                    load_x(g + 3, (g + 1) % 2)
                sp.wait_ge(out_ready, s - GS)
                store_out(g - 2, g % 2)
            for g in range(GROUPS, GROUPS + 2):
                sp.wait_ge(out_ready, GS * (g - 1))
                store_out(g - 2, g % 2)
            for c in range(2):
                sp.wait_ge(out_stored[c], 16 * GROUPS // 2)

        @block.tensor
        def _(pe):
            def turn_x(slot):
                nc.tensor.transpose(xT_ps, x_rows[:, slot, :], ident[:, :]).then_inc(x_turned, GS)

            def bias0(c):
                nc.tensor.matmul(a0_group(c), bias_lhs[:, :],
                                 pick[:, 1:NG].unsqueeze(1).unsqueeze(3).to_broadcast([P, GS, 3, N]),
                                 start=True, stop=False, skip_group_check=True)
                nc.tensor.matmul(ao_group(c), bias_lhs[:, :],
                                 pick[:, 0:1].unsqueeze(1).to_broadcast([P, GS, N]),
                                 start=True, stop=False, skip_group_check=True)

            def project0(c, q):
                nc.tensor.matmul(ao_group(c) if q == GATE_O else a0_group(c)[:, :, IFG.index(q), :],
                                 wx_s[:, q, :], xT[:, c, :, :], start=False, stop=False, skip_group_check=True)

            def bias1(c):
                nc.tensor.matmul(a1[c][:, 0:GS * 2 * N].rearrange("p (t g n) -> p t g n", t=GS, g=2),
                                 bias_lhs[:, :],
                                 pick[:, NG:NG + 2].unsqueeze(1).unsqueeze(3).to_broadcast([P, GS, 2, N]),
                                 start=True, stop=False, skip_group_check=True)

            def project1(c, q):
                nc.tensor.matmul(a1[c][:, 0:GS * 2 * N].rearrange("p (t g n) -> p t g n", t=GS, g=2)[:, :, q, :],
                                 w1x_s[:, q, :], x1T[:, c, :, :], start=False, stop=False,
                                 skip_group_check=True)

            PRODUCTS = ((0, 1, 2), (0, 1), (0,))

            def layer0(s, j):
                prev = (j - 1) % BODY
                moving = (upper(hT[:, prev, :]), upper(h_rest[:, prev % 2, :]), h_low[:, prev % 2, :])

                def products(part, gates):
                    for q in gates:
                        o = IFG.index(q) * N if q != GATE_O else 0
                        to = ao_step(j) if q == GATE_O else a0_step(j)[:, o:o + N]
                        for w in PRODUCTS[part]:
                            mm = nc.tensor.matmul(to, wh_part[:, w, q * P:(q + 1) * P], moving[part],
                                                  start=False, stop=(part == 2), skip_group_check=True)
                    return mm

                pe.wait_ge(h_ready, s + 1)
                products(0, IFG)
                pe.wait_ge(h_rest_ready, s + 1)
                products(1, IFG)
                products(0, (GATE_O,))
                pe.wait_ge(h_low_ready, s + 1)
                products(2, IFG).then_inc(ifg_summed, 1)
                products(1, (GATE_O,))
                products(2, (GATE_O,)).then_inc(o_summed, 1)

            def layer1(part, r, j):
                prev = (j - 1) % BODY
                moving = (upper(u_of(prev)), upper(u_rest[:, prev % 2, :]), u_low[:, prev % 2, :])[part]
                pe.wait_ge((u_ready, u_rest_ready, u_low_ready)[part], r + 1)
                for q in range(2):
                    for w in PRODUCTS[part]:
                        mm = nc.tensor.matmul(a1_step(j)[:, q * N:(q + 1) * N],
                                              w1h_part[:, w, q * P:(q + 1) * P], moving,
                                              start=False, stop=(part == 2), skip_group_check=True)
                if part == 2:
                    mm.then_inc(a1_summed, 1)

            def start_layer1_group(r, c):
                pe.wait_ge(x1_ready, r + GS)
                bias1(c)
                project1(c, 0)
                project1(c, 1)

            pe.wait_ge(ident_ready, 1)
            pe.wait_ge(cond_in, 16)
            nc.tensor.transpose(cell_ps[:, 0:N], cond_rows[:, :], ident[0:N, 0:N]).then_inc(cond_turned, 1)
            pe.wait_ge(x_in[0], 16)
            turn_x(0)
            pe.wait_ge(bias_ready, 1)
            bias0(0)
            pe.wait_ge(wx_ready, 1)
            pe.wait_ge(xT_ready, GS)
            for q in range(NG):
                project0(0, q)
            pe.wait_ge(weights_split, SPLIT_STAGES)

            def body(s0, first, last):
                for j in range(BODY):
                    s, c, k = s0 + j, j // GS, j % GS
                    other = (c + 1) % 2
                    more = not (last and c == 1)
                    layer0(s, j)
                    if k == 0 and more:
                        pe.wait_ge(x_in[other], 16 // BODY * (s0 + (1 if c else 0) * BODY + BODY) if c else
                                   16 // BODY * (s0 + BODY))
                        turn_x(other)
                    if k == 0 and not (first and c == 0):
                        if first:
                            pe.wait_ge(weights_split, 2 * SPLIT_STAGES)
                        start_layer1_group(s - LAG, other)
                    r, l = s - LAG, (j - LAG) % BODY
                    two = not (first and c == 0)
                    if k == 1 and more:
                        bias0(other)
                    if k == 2 and more:
                        project0(other, GATE_F)
                    if k == 3 and more:
                        project0(other, GATE_G)
                    if two:
                        layer1(0, r, l)
                    if k == 1 and more:
                        pe.wait_ge(xT_ready, s - 1 + 2 * GS)
                        project0(other, GATE_I)
                    if k == 3 and more:
                        project0(other, GATE_O)
                    if two:
                        layer1(1, r, l)
                        layer1(2, r, l)
                    if k == 1 and not first:
                        pe.wait_ge(sum_ready, s - 1 - GS)
                        nc.tensor.transpose(out_ps, sumT[:, :, :].rearrange("p t n -> p (t n)"),
                                            ident[:, :]).then_inc(out_turned, GS)

            schedule(pe, body)
            start_layer1_group(T - LAG, 1)
            for k in range(GS):
                for part in range(3):
                    layer1(part, T - LAG + k, GS + k)
            for g in range(GROUPS, GROUPS + 2):
                pe.wait_ge(sum_ready, GS * (g - 1))
                if g > GROUPS:
                    pe.wait_ge(out_ready, GS * (g - 2))
                nc.tensor.transpose(out_ps, sumT[:, :, :].rearrange("p t n -> p (t n)"),
                                    ident[:, :]).then_inc(out_turned, GS)

        @block.scalar
        def _(act):
            def copy_xT(c, count):
                act.wait_ge(x_turned, count)
                nc.scalar.activation(xT[:, c, :, :].rearrange("p t n -> p (t n)"), xT_ps,
                                     ACT.Copy).then_inc(xT_ready, GS)

            def copy_out(c, count, stored):
                act.wait_ge(out_turned, count)
                if stored is not None:
                    act.wait_ge(out_stored[c], stored)
                nc.scalar.activation(out_rows[:, c, :], out_ps, ACT.Copy).then_inc(out_ready, GS)

            def layer0(s, j):
                act.wait_ge(ifg_summed, s + 1)
                nc.scalar.activation(acts[:, j % 2, N:NG * N], a0_step(j),
                                     ACT.Tanh).then_inc(ifg_ready, 1)
                act.wait_ge(o_summed, s + 1)
                nc.scalar.activation(acts[:, j % 2, 0:N], ao_step(j), ACT.Tanh).then_inc(o_ready, 1)
                act.wait_ge(cell_ready, 2 * s + 1)
                nc.scalar.activation(tanh_c[:, j % 2, :], cell_ps[:, (j % 2) * N:(j % 2 + 1) * N], ACT.Tanh,
                                     scale=0.5).then_inc(tanh_c_ready, 1)

            def layer1(r, j):
                b = j % BODY
                act.wait_ge(a1_summed, r + 1)
                nc.scalar.activation(acts1[:, b, 0:4:3, :], a1_step(j).rearrange("p (g n) -> p g n", g=2),
                                     ACT.Tanh)
                nc.scalar.activation(acts1[:, b, 1, :], a1_step(j)[:, 0:N], ACT.Tanh,
                                     scale=-1.0).then_inc(acts1_ready, 1)

            act.dma_start(wh_raw[:, :], wh).then_inc(wh_in, 16)
            act.dma_start(cond_rows[:, :], h_first).then_inc(cond_in, 16)
            act.wait_ge(blank_ready, 1)
            nc.scalar.activation(acts_blank[:, :], acts_blank[:, :], ACT.Tanh)
            copy_xT(0, GS)
            act.wait_ge(wx_in, 16)
            nc.scalar.activation(wx_s[:, 0:SIGMOIDS, :].rearrange("p g n -> p (g n)"), wx_raw[:, 0:SIGMOIDS * P],
                                 ACT.Copy, scale=0.5)
            nc.scalar.activation(wx_s[:, GATE_G, :], wx_raw[:, GATE_G * P:NG * P], ACT.Copy).then_inc(wx_ready, 1)

            def body(s0, first, last):
                for j in range(BODY):
                    s, c, k = s0 + j, j // GS, j % GS
                    layer0(s, j)
                    if not (first and c == 0):
                        layer1(s - LAG, (j - LAG) % BODY)
                    if k == 0 and not (last and c == 1):
                        copy_xT((c + 1) % 2, s + 2 * GS)
                    if k == 2 and not first:
                        copy_out(c, s - 2 - GS, 16 // BODY * (s0 - BODY))

            body(0, True, False)
            for j in range(BODY):
                s, c, k = BODY + j, j // GS, j % GS
                layer0(s, j)
                layer1(s - LAG, (j - LAG) % BODY)
                if k == 0:
                    copy_xT((c + 1) % 2, s + 2 * GS)
                if k == 2:
                    copy_out(c, s - 2 - GS, None)
            with act.Fori(2 * BODY, T - BODY, BODY) as s0:
                body(s0, False, False)
            body(T - BODY, False, True)
            for k in range(GS):
                layer1(T - LAG + k, GS + k)
            for g in range(GROUPS, GROUPS + 2):
                copy_out(g % 2, GS * (g - 1), 16 * (g // 2 - 1))

        @block.vector
        def _(dve):
            steps = [0]

            def then(ins):
                steps[0] += 1
                ins.then_inc(bias_step, 1)
                dve.wait_ge(bias_step, steps[0])

            def layer0_products(s, j):
                b = j % 2
                dve.wait_ge(ifg_ready, s + 1)
                nc.vector.scalar_tensor_tensor(out=pair[:, :], in0=acts[:, b, N:3 * N], scalar=1.0,
                                               in1=acts[:, b, 3 * N:5 * N], op0=ALU.add,
                                               op1=ALU.mult).then_inc(pair_ready, 1)

            def layer0_cell(s, j):
                dve.wait_ge(pair_ready, s + 1)
                for cell in (cell_ps[:, j % 2 * N:(j % 2 + 1) * N], acts[:, (j + 1) % 2, NG * N:(NG + 1) * N]):
                    nc.vector.scalar_tensor_tensor(out=cell, in0=pair[:, N:2 * N], scalar=0.5,
                                                   in1=pair[:, 0:N], op0=ALU.mult,
                                                   op1=ALU.add).then_inc(cell_ready, 1)

            def layer0_state(s, j):
                dve.wait_ge(tanh_c_ready, s + 1)
                nc.vector.scalar_tensor_tensor(out=hT[:, j, :], in0=acts[:, j % 2, 0:N], scalar=1.0,
                                               in1=tanh_c[:, j % 2, :], op0=ALU.add,
                                               op1=ALU.mult).then_inc(h_ready, 1)

            def split_h(s, j):
                dve.wait_ge(h_ready, s + 2)
                nc.vector.tensor_tensor(h_rest[:, j % 2, :], hT[:, j % BODY, :], upper(hT[:, j % BODY, :]),
                                        ALU.subtract).then_inc(h_rest_ready, 1)
                dve.wait_ge(h_rest_ready, s + 2)
                nc.vector.tensor_tensor(h_low[:, j % 2, :], h_rest[:, j % 2, :], upper(h_rest[:, j % 2, :]),
                                        ALU.subtract).then_inc(h_low_ready, 1)

            def layer1(r, j):
                b = j % BODY
                dve.wait_ge(acts1_ready, r + 1)
                nc.vector.scalar_tensor_tensor(out=pair1[:, :, :], in0=acts1[:, b, 0:2, :], scalar=1.0,
                                               in1=acts1[:, b, 2:4, :], op0=ALU.add,
                                               op1=ALU.mult).then_inc(pair1_ready, 1)
                dve.wait_ge(pair1_ready, r + 1)
                nc.vector.scalar_tensor_tensor(out=u_of(j), in0=pair1[:, 0, :], scalar=0.5,
                                               in1=pair1[:, 1, :], op0=ALU.mult,
                                               op1=ALU.add).then_inc(u_ready, 1)
                split_u_high(r, j)

            def split_u_high(r, j):
                dve.wait_ge(u_ready, r + 2)
                nc.vector.tensor_tensor(u_rest[:, j % 2, :], u_of(j), upper(u_of(j)),
                                        ALU.subtract).then_inc(u_rest_ready, 1)

            def split_u_low(r, j):
                dve.wait_ge(u_rest_ready, r + 2)
                nc.vector.tensor_tensor(u_low[:, j % 2, :], u_rest[:, j % 2, :], upper(u_rest[:, j % 2, :]),
                                        ALU.subtract).then_inc(u_low_ready, 1)

            def add_layer0(c, t0, t1):
                return nc.vector.scalar_tensor_tensor(
                    out=x1T[:, c, t0:t1, :].rearrange("p t n -> p (t n)"),
                    in0=hT[:, c * GS + t0:c * GS + t1, :].rearrange("p t n -> p (t n)"), scalar=0.5,
                    in1=xT[:, c, t0:t1, :].rearrange("p t n -> p (t n)"), op0=ALU.mult, op1=ALU.add)

            def add_layer1(c, count):
                dve.wait_ge(u_ready, count + 1)
                runs = [(0, GS)] if c == 0 else [(0, GS - 1), (GS - 1, GS)]
                for t0, t1 in runs:
                    j = c * GS + t0 + 1
                    ins = nc.vector.scalar_tensor_tensor(
                        out=sumT[:, t0:t1, :], in0=acts1[:, j % BODY:j % BODY + t1 - t0, 2, :], scalar=0.5,
                        in1=x1T[:, c, t0:t1, :], op0=ALU.mult, op1=ALU.add)
                ins.then_inc(sum_ready, GS)

            def split_weights(stage, parts, rest, raw, runs, done):
                dve.wait_ge(weights_split, done) if done else None
                if stage == 0:
                    for a, b, factor in runs:
                        ins = nc.vector.tensor_scalar(parts[:, 0, a:b], raw[:, a:b], factor, None, ALU.mult)
                elif stage == 1:
                    for a, b, factor in runs:
                        ins = nc.vector.scalar_tensor_tensor(out=rest[:, a:b], in0=raw[:, a:b], scalar=factor,
                                                             in1=parts[:, 0, a:b], op0=ALU.mult,
                                                             op1=ALU.subtract)
                elif stage == 2:
                    ins = nc.vector.tensor_copy(parts[:, 1, :], rest[:, :])
                else:
                    ins = nc.vector.tensor_tensor(parts[:, 2, :], rest[:, :], parts[:, 1, :], ALU.subtract)
                ins.then_inc(weights_split, 1)

            nc.vector.memset(acts_blank[:, :], 0.0).then_inc(blank_ready, 1)
            nc.vector.memset(acts[:, 0, NG * N:(NG + 1) * N], 0.0)
            then(nc.vector.memset(bias_lhs[:, :], 0.0))
            dve.wait_ge(ident_ready, 1)
            then(nc.vector.tensor_tensor(pick_sum[:, :], ident[:, 0:NG + 2], ident[:, QUADRANT:QUADRANT + NG + 2],
                                         ALU.add))
            then(nc.vector.tensor_tensor(pick_sum[:, :], pick_sum[:, :],
                                         ident[:, 2 * QUADRANT:2 * QUADRANT + NG + 2], ALU.add))
            then(nc.vector.tensor_tensor(pick_sum[:, NG:NG + 1], pick_sum[:, NG:NG + 1],
                                         ident[:, ONE_ROW:ONE_ROW + 1], ALU.add))
            nc.vector.tensor_scalar(pick[:, 0:1], pick_sum[:, GATE_O:GATE_O + 1], 0.5, None, ALU.mult)
            nc.vector.tensor_scalar(pick[:, 1:3], pick_sum[:, GATE_I:GATE_F + 1], 0.5, None, ALU.mult)
            nc.vector.tensor_copy(pick[:, 3:4], pick_sum[:, GATE_G:GATE_G + 1])
            nc.vector.tensor_scalar(pick[:, 4:5], pick_sum[:, 4:5], 0.5, None, ALU.mult)
            nc.vector.tensor_copy(pick[:, 5:6], pick_sum[:, 5:6])
            dve.wait_ge(cond_turned, 1)
            nc.vector.tensor_scalar(hT[:, BODY - 1, :], cell_ps[:, 0:N], 2.0, None, ALU.mult).then_inc(h_ready, 1)
            nc.vector.tensor_scalar(u_of(BODY - 1), cell_ps[:, 0:N], 2.0, None, ALU.mult).then_inc(u_ready, 1)
            split_h(-1, BODY - 1)
            split_u_high(-1, BODY - 1)
            split_u_low(-1, BODY - 1)
            dve.wait_ge(wh_in, 16)
            for stage in range(SPLIT_STAGES):
                split_weights(stage, wh_part, wh_rest, wh_raw,
                              ((0, SIGMOIDS * P, 0.25), (SIGMOIDS * P, NG * P, 0.5)), stage)
            dve.wait_ge(rows_zero, 1)
            dve.wait_ge(b_in, 16 * 6)
            then(nc.vector.tensor_copy(bias_lhs[0:3 * QUADRANT, :], bias_rows[0:3 * QUADRANT, :]))
            then(nc.vector.tensor_tensor(bias_rest[0:2 * QUADRANT, :], bias_rows[0:2 * QUADRANT, :],
                                         bias_lhs[0:2 * QUADRANT, :], ALU.subtract))
            then(nc.vector.tensor_copy(bias_lhs[0:2 * QUADRANT, :], bias_rest[0:2 * QUADRANT, :]))
            then(nc.vector.tensor_tensor(bias_rest[0:QUADRANT, :], bias_rest[0:QUADRANT, :],
                                         bias_lhs[0:QUADRANT, :], ALU.subtract))
            nc.vector.tensor_copy(bias_lhs[0:QUADRANT, :], bias_rest[0:QUADRANT, :]).then_inc(bias_ready, 1)

            def layer1_weights(stage):
                if stage == 0:
                    dve.wait_ge(w1_in, 16)
                    nc.vector.tensor_scalar(w1x_s[:, 0, :], w1_raw[:, 0, 0:P], 0.5, None, ALU.mult)
                    nc.vector.tensor_copy(w1x_s[:, 1, :], w1_raw[:, 0, P:2 * P])
                split_weights(stage, w1h_part, w1h_rest, w1_raw[:, 1, :], ((0, P, 0.25), (P, 2 * P, 0.5)),
                              SPLIT_STAGES + stage)

            def body(s0, first, last):
                for j in range(BODY):
                    s, c, k = s0 + j, j // GS, j % GS
                    two = not (first and c == 0)
                    r, l = s - LAG, (j - LAG) % BODY
                    layer0_products(s, j)
                    if two and not (first and j == GS):
                        split_u_low(r - 1, (l - 1) % BODY)
                    layer0_cell(s, j)
                    if k == 0 and not first:
                        add_layer1(c, s - GS)
                    if k == 3:
                        dve.wait_ge(xT_ready, s + 1)
                        dve.wait_ge(h_ready, s + 1)
                        add_layer0(c, 0, GS - 1)
                    layer0_state(s, j)
                    split_h(s, j)
                    if k == 3:
                        add_layer0(c, GS - 1, GS).then_inc(x1_ready, GS)
                    if two:
                        layer1(r, l)
                    else:
                        layer1_weights(k)

            schedule(dve, body)
            for k in range(GS):
                split_u_low(T - LAG + k - 1, GS + k - 1)
                if k == 0:
                    add_layer1(0, T - GS)
                layer1(T - LAG + k, GS + k)
            dve.wait_ge(out_turned, T - GS)
            add_layer1(1, T)


_INS = ["x", "cond_1024", "L0_cond_Wx", "L0_cond_Wh", "L0_cond_b", "L1_cond_weight", "L1_cond_bias"]


def kernel(**inputs):
    import numpy as _np
    import concourse.bacc as _bacc
    from concourse import mybir as _mybir
    from concourse.bass_utils import run_bass_kernel_spmd as _run

    nc = _bacc.Bacc("TRN2", target_bir_lowering=False, num_devices=1)
    arrays, args = {}, []
    for name in _INS:
        a = _np.ascontiguousarray(inputs[name])
        arrays[f"in_{name}_dram"] = a
        args.append(nc.dram_tensor(f"in_{name}_dram", a.shape, _mybir.dt.from_np(a.dtype), kind="ExternalInput").ap())
    shape = inputs["x"].shape
    out = nc.dram_tensor("out_0_dram", shape, F32, kind="ExternalOutput").ap()
    two_layer_recurrence(nc, *args, out)
    r = _run(nc, [arrays], core_ids=[0])
    return r.results[0]["out_0_dram"]
```

```python
import concourse.bass as bass
from concourse import mybir
from contextlib import ExitStack

F32 = mybir.dt.float32
BF16 = mybir.dt.bfloat16
ALU = mybir.AluOpType
ACT = mybir.ActivationFunctionType

P = 128
N = 32
T = 128
GS = 4
GROUPS = T // GS
RING = 2 * GS
BODY = 2 * RING
QUADRANT = 32
SPLIT_STAGES = 4
ONE_ROW = 3 * QUADRANT
LAG = GS

GATE_I, GATE_F, GATE_O, GATE_G = range(4)
NG = 4
IFG = (GATE_I, GATE_F, GATE_G)
SIGMOIDS = 3


def two_layer_recurrence(nc, x, h_first, wx, wh, b0, w1, b1, out):
    x_g = x.rearrange("n (g t) d -> g t n d", t=GS)
    out_g = out.rearrange("n (g t) d -> g t n d", t=GS)
    ctx = ExitStack()
    with ctx:
        def sb(name, shape, dt=F32):
            return ctx.enter_context(nc.sbuf_tensor(name, shape, dt))

        def bank(name):
            return ctx.enter_context(nc.psum_tensor(name, [P, 512], F32))

        def sem(name):
            return ctx.enter_context(nc.semaphore(name))

        x_rows = sb("x_rows", [P, 2, P])
        cond_rows = sb("cond_rows", [N, P])
        wx_raw = sb("wx_raw", [P, NG * P])
        wh_raw = sb("wh_raw", [P, NG * P])
        w1_raw = sb("w1_raw", [P, 2, 2 * P])
        bias_rows = sb("bias_rows", [NG + 2, P])
        wx_s = sb("wx_s", [P, NG, P])
        w1x_s = sb("w1x_s", [P, 2, P])
        wh_rest = sb("wh_rest", [P, NG * P])
        wh_part = sb("wh_part", [P, 3, NG * P], BF16)
        w1h_rest = sb("w1h_rest", [P, 2 * P])
        w1h_part = sb("w1h_part", [P, 3, 2 * P], BF16)
        bias_rest = sb("bias_rest", [NG + 2, P])
        bias_lhs = sb("bias_lhs", [P, P], BF16)
        pick_sum = sb("pick_sum", [P, NG + 2])
        pick = sb("pick", [P, NG + 2], BF16)
        ident = sb("ident", [P, P])
        xT = sb("xT", [P, 2, GS, N])
        x1T = sb("x1T", [P, 2, GS, N])
        hT = sb("hT", [P, RING, N])
        h_rest = sb("h_rest", [P, 2, N])
        h_low = sb("h_low", [P, 2, N], BF16)
        sumT = sb("sumT", [P, GS, N])
        acts = sb("acts", [P, 2, (NG + 1) * N])
        acts_blank = sb("acts_blank", [P, 1])
        pair = sb("pair", [P, 2 * N])
        tanh_c = sb("tanh_c", [P, 2, N])
        acts1 = sb("acts1", [P, RING, 4, N])
        pair1 = sb("pair1", [P, 2, N])
        u_rest = sb("u_rest", [P, 2, N])
        u_low = sb("u_low", [P, 2, N], BF16)
        out_rows = sb("out_rows", [P, 2, P])

        a0 = [bank(f"a0_{i}") for i in range(2)]
        ao = [bank(f"ao_{i}") for i in range(2)]
        a1 = [bank(f"a1_{i}") for i in range(2)]
        turned_ps = bank("turned_ps")
        xT_ps, out_ps = turned_ps[:, 0:P], turned_ps[:, P:2 * P]
        cell_ps = bank("cell_ps")

        x_in = [sem(f"x_in{i}") for i in range(2)]
        cond_in = sem("cond_in")
        wx_in, wh_in, w1_in, b_in = sem("wx_in"), sem("wh_in"), sem("w1_in"), sem("b_in")
        out_stored = [sem(f"out_stored{i}") for i in range(2)]
        ident_zero, ident_ready = sem("ident_zero"), sem("ident_ready")
        wx_ready = sem("wx_ready")
        weights_split = sem("weights_split")
        setup_step, pick_ready = sem("setup_step"), sem("pick_ready")
        bias_ready = sem("bias_ready")
        cond_turned = sem("cond_turned")
        ifg_summed, o_summed = sem("ifg_summed"), sem("o_summed")
        ifg_ready = sem("ifg_ready")
        pair_ready, tanh_c_ready = sem("pair_ready"), sem("tanh_c_ready")
        cell_ready = sem("cell_ready")
        h_ready = sem("h_ready")
        a1_summed, acts1_ready = sem("a1_summed"), sem("acts1_ready")
        h_rest_ready, h_low_ready = sem("h_rest_ready"), sem("h_low_ready")
        pair1_ready = sem("pair1_ready")
        u_ready, u_rest_ready, u_low_ready = sem("u_ready"), sem("u_rest_ready"), sem("u_low_ready")
        blank_ready = sem("blank_ready")
        x_turned, xT_ready, x1_ready = sem("x_turned"), sem("xT_ready"), sem("x1_ready")
        x1_early = sem("x1_early")
        sum_ready, out_turned, out_ready = sem("sum_ready"), sem("out_turned"), sem("out_ready")

        block = ctx.enter_context(nc.Block())

        def upper(ap):
            return ap.bitcast(BF16).rearrange("p (n two) -> p n two", two=2)[:, :, 1]

        def u_of(j):
            return acts1[:, (j + 1) % RING, 2, :]

        def a0_group(c):
            return a0[c][:, 0:GS * 3 * N].rearrange("p (t g n) -> p t g n", t=GS, g=3)

        def ao_group(c):
            return ao[c][:, 0:GS * N].rearrange("p (t n) -> p t n", t=GS)

        def a0_step(j):
            o = (j % GS) * 3 * N
            return a0[j // GS % 2][:, o:o + 3 * N]

        def ao_step(j):
            o = (j % GS) * N
            return ao[j // GS % 2][:, o:o + N]

        def a1_step(j):
            o = (j % GS) * 2 * N
            return a1[j // GS % 2][:, o:o + 2 * N]

        def place(j):
            return j // GS, j // GS % 2, j % GS

        def schedule(eng, body):
            body(0, True, False)
            with eng.Fori(BODY, T - BODY, BODY) as s0:
                body(s0, False, False)
            body(T - BODY, False, True)

        @block.gpsimd
        def _(pool):
            nc.gpsimd.memset(ident[:, :], 0.0).then_inc(ident_zero, 1)
            pool.wait_ge(ident_zero, 1)
            nc.gpsimd.affine_select(out=ident[:, :], in_=ident[:, :], compare_op=ALU.not_equal, fill=1.0,
                                    base=0, pattern=[[-1, P]], channel_multiplier=1).then_inc(ident_ready, 1)
            last = RING - 1
            pool.wait_ge(h_ready, 1)
            nc.gpsimd.tensor_tensor(h_rest[:, last % 2, :], hT[:, last, :], upper(hT[:, last, :]),
                                    ALU.subtract).then_inc(h_rest_ready, 1)
            pool.wait_ge(h_rest_ready, 1)
            nc.gpsimd.tensor_tensor(h_low[:, last % 2, :], h_rest[:, last % 2, :], upper(h_rest[:, last % 2, :]),
                                    ALU.subtract).then_inc(h_low_ready, 1)
            pool.wait_ge(u_ready, 1)
            nc.gpsimd.tensor_tensor(u_rest[:, last % 2, :], u_of(last), upper(u_of(last)),
                                    ALU.subtract).then_inc(u_rest_ready, 1)
            pool.wait_ge(u_rest_ready, 1)
            nc.gpsimd.tensor_tensor(u_low[:, last % 2, :], u_rest[:, last % 2, :], upper(u_rest[:, last % 2, :]),
                                    ALU.subtract).then_inc(u_low_ready, 1)

        @block.sync
        def _(sp):
            def load_x(g, slot):
                sp.dma_start(x_rows[:, slot, :], x_g[g]).then_inc(x_in[slot], 16)

            def store_out(g, slot):
                sp.dma_start(out_g[g], out_rows[:, slot, :]).then_inc(out_stored[slot], 16)

            load_x(0, 0)
            sp.dma_start(wx_raw[:, :], wx).then_inc(wx_in, 16)
            sp.dma_start(bias_rows[0:NG, :], b0.rearrange("(g n) -> g n", n=P)).then_inc(b_in, 16)
            sp.dma_start(bias_rows[NG:NG + 2, :], b1.rearrange("(g n) -> g n", n=P)).then_inc(b_in, 16)
            sp.dma_start(cond_rows[:, :], h_first).then_inc(cond_in, 16)
            load_x(1, 1)
            sp.dma_start(w1_raw[:, :, :], w1.rearrange("(h k) n -> k h n", h=2)).then_inc(w1_in, 16)
            sp.wait_ge(x_turned, GS)
            load_x(2, 0)

            def group(g, slot, load, store):
                if load:
                    sp.wait_ge(x_turned, (g + 2) * GS)
                    load_x(g + 3, 1 - slot)
                if store:
                    sp.wait_ge(out_ready, (g - 1) * GS)
                    store_out(g - 2, slot)

            for slot in range(2):
                group(slot, slot, True, False)
            with sp.Fori(1, GROUPS // 2 - 2) as both:
                for slot in range(2):
                    group(both * 2 + slot, slot, True, True)
            for g in range(GROUPS - 4, GROUPS):
                group(g, g % 2, g + 3 < GROUPS, True)
            for g in range(GROUPS, GROUPS + 2):
                sp.wait_ge(out_ready, GS * (g - 1))
                store_out(g - 2, g % 2)
            for c in range(2):
                sp.wait_ge(out_stored[c], 16 * GROUPS // 2)

        @block.tensor
        def _(pe):
            def turn_x(slot):
                nc.tensor.transpose(xT_ps, x_rows[:, slot, :], ident[:, :]).then_inc(x_turned, GS)

            def bias0(c, start=True):
                nc.tensor.matmul(a0_group(c), bias_lhs[:, :],
                                 pick[:, 1:NG].unsqueeze(1).unsqueeze(3).to_broadcast([P, GS, 3, N]),
                                 start=start, stop=False, skip_group_check=True)
                nc.tensor.matmul(ao_group(c), bias_lhs[:, :],
                                 pick[:, 0:1].unsqueeze(1).to_broadcast([P, GS, N]),
                                 start=start, stop=False, skip_group_check=True)

            def project0(c, q, start=False):
                nc.tensor.matmul(ao_group(c) if q == GATE_O else a0_group(c)[:, :, IFG.index(q), :],
                                 wx_s[:, q, :], xT[:, c, :, :], start=start, stop=False, skip_group_check=True)

            def bias1(c):
                nc.tensor.matmul(a1[c][:, 0:GS * 2 * N].rearrange("p (t g n) -> p t g n", t=GS, g=2),
                                 bias_lhs[:, :],
                                 pick[:, NG:NG + 2].unsqueeze(1).unsqueeze(3).to_broadcast([P, GS, 2, N]),
                                 start=True, stop=False, skip_group_check=True)

            def project1(c, q, t0=0, t1=GS):
                nc.tensor.matmul(a1[c][:, 0:GS * 2 * N].rearrange("p (t g n) -> p t g n", t=GS, g=2)[:, t0:t1, q, :],
                                 w1x_s[:, q, :], x1T[:, c, t0:t1, :], start=False, stop=False,
                                 skip_group_check=True)

            PRODUCTS = ((0, 1, 2), (0, 1), (0,))

            def layer0(s, j):
                prev = (j - 1) % RING
                moving = (upper(hT[:, prev, :]), upper(h_rest[:, prev % 2, :]), h_low[:, prev % 2, :])

                def products(part, gates, weights=None):
                    for q in gates:
                        o = IFG.index(q) * N if q != GATE_O else 0
                        to = ao_step(j) if q == GATE_O else a0_step(j)[:, o:o + N]
                        for w in weights or PRODUCTS[part]:
                            mm = nc.tensor.matmul(to, wh_part[:, w, q * P:(q + 1) * P], moving[part],
                                                  start=False, stop=(part == 2), skip_group_check=True)
                    return mm

                pe.wait_ge(h_ready, s + 1)
                products(0, IFG)
                pe.wait_ge(h_rest_ready, s + 1)
                products(1, IFG)
                products(0, (GATE_O,), weights=(0, 1))
                pe.wait_ge(h_low_ready, s + 1)
                products(2, IFG).then_inc(ifg_summed, 1)
                products(0, (GATE_O,), weights=(2,))
                products(1, (GATE_O,))
                products(2, (GATE_O,)).then_inc(o_summed, 1)

            def layer1(part, r, j):
                prev = (j - 1) % RING
                moving = (upper(u_of(prev)), upper(u_rest[:, prev % 2, :]), u_low[:, prev % 2, :])[part]
                pe.wait_ge((u_ready, u_rest_ready, u_low_ready)[part], r + 1)
                for q in range(2):
                    for w in PRODUCTS[part]:
                        mm = nc.tensor.matmul(a1_step(j)[:, q * N:(q + 1) * N],
                                              w1h_part[:, w, q * P:(q + 1) * P], moving,
                                              start=False, stop=(part == 2), skip_group_check=True)
                if part == 2:
                    mm.then_inc(a1_summed, 1)

            pe.wait_ge(ident_ready, 1)
            pe.wait_ge(x_in[0], 16)
            turn_x(0)
            pe.wait_ge(cond_in, 16)
            nc.tensor.transpose(cell_ps[:, 0:N], cond_rows[:, :], ident[0:N, 0:N]).then_inc(cond_turned, 1)
            pe.wait_ge(wx_ready, 1)
            pe.wait_ge(xT_ready, GS)
            for q in range(NG):
                project0(0, q, start=q in (GATE_I, GATE_O))
            pe.wait_ge(bias_ready, 1)
            pe.wait_ge(pick_ready, 1)
            bias0(0, start=False)
            pe.wait_ge(weights_split, SPLIT_STAGES)

            def body(s0, first, last):
                for j in range(BODY):
                    s, (m, c, k) = s0 + j, place(j)
                    other = (c + 1) % 2
                    more = not (last and m == BODY // GS - 1)
                    two = not (first and m == 0)
                    r, l = s - LAG, (j - LAG) % RING
                    layer0(s, j)
                    if k == 0 and two:
                        if first and m == 1:
                            pe.wait_ge(weights_split, 2 * SPLIT_STAGES)
                        pe.wait_ge(x1_ready, s)
                        project1(other, 0)
                        project1(other, 1)
                    if k == 1:
                        bias1(c)
                        if more:
                            pe.wait_ge(x_in[other], 2 * s0 + 16 * ((m + 1) // 2 + 1))
                            turn_x(other)
                    if k == 2 and more:
                        pe.wait_ge(xT_ready, s - 2 + 2 * GS)
                        project0(other, GATE_I)
                    if k == 3 and more:
                        project0(other, GATE_G)
                    if two:
                        layer1(0, r, l)
                    if k == 1 and more:
                        bias0(other)
                    if k == 2 and more:
                        project0(other, GATE_F)
                    if k == 3 and more:
                        project0(other, GATE_O)
                    if two:
                        layer1(1, r, l)
                        layer1(2, r, l)
                    if k == 3 and not more:
                        pe.wait_ge(x1_early, 1)
                        project1(1, 0, 0, GS - 1)
                        project1(1, 1, 0, GS - 1)
                    if k == 2 and not (first and m < 2):
                        pe.wait_ge(sum_ready, s - 2 - GS)
                        nc.tensor.transpose(out_ps, sumT[:, :, :].rearrange("p t n -> p (t n)"),
                                            ident[:, :]).then_inc(out_turned, GS)

            schedule(pe, body)
            pe.wait_ge(x1_ready, T)
            project1(1, 0, GS - 1, GS)
            project1(1, 1, GS - 1, GS)
            for k in range(GS):
                for part in range(3):
                    layer1(part, T - LAG + k, GS + k)
            for g in range(GROUPS, GROUPS + 2):
                pe.wait_ge(sum_ready, GS * (g - 1))
                if g > GROUPS:
                    pe.wait_ge(out_ready, GS * (g - 2))
                nc.tensor.transpose(out_ps, sumT[:, :, :].rearrange("p t n -> p (t n)"),
                                    ident[:, :]).then_inc(out_turned, GS)

        @block.scalar
        def _(act):
            def copy_xT(c, count):
                act.wait_ge(x_turned, count)
                nc.scalar.activation(xT[:, c, :, :].rearrange("p t n -> p (t n)"), xT_ps,
                                     ACT.Copy).then_inc(xT_ready, GS)

            def copy_out(c, count, stored):
                act.wait_ge(out_turned, count)
                if stored is not None:
                    act.wait_ge(out_stored[c], stored)
                nc.scalar.activation(out_rows[:, c, :], out_ps, ACT.Copy).then_inc(out_ready, GS)

            def layer0(s, j):
                act.wait_ge(ifg_summed, s + 1)
                nc.scalar.activation(acts[:, j % 2, N:NG * N], a0_step(j),
                                     ACT.Tanh).then_inc(ifg_ready, 1)
                act.wait_ge(o_summed, s + 1)
                nc.scalar.activation(acts[:, j % 2, 0:N], ao_step(j), ACT.Tanh)
                act.wait_ge(cell_ready, 2 * s + 1)
                nc.scalar.activation(tanh_c[:, j % 2, :], cell_ps[:, (j % 2) * N:(j % 2 + 1) * N], ACT.Tanh,
                                     scale=0.5).then_inc(tanh_c_ready, 1)

            def layer1(r, j):
                b = j % RING
                act.wait_ge(a1_summed, r + 1)
                nc.scalar.activation(acts1[:, b, 0:4:3, :], a1_step(j).rearrange("p (g n) -> p g n", g=2),
                                     ACT.Tanh)
                nc.scalar.activation(acts1[:, b, 1, :], a1_step(j)[:, 0:N], ACT.Tanh,
                                     scale=-1.0).then_inc(acts1_ready, 1)

            act.dma_start(wh_raw[:, :], wh).then_inc(wh_in, 16)
            act.wait_ge(blank_ready, 1)
            nc.scalar.activation(acts_blank[:, :], acts_blank[:, :], ACT.Tanh)
            copy_xT(0, GS)
            act.wait_ge(wx_in, 16)
            nc.scalar.activation(wx_s[:, 0:SIGMOIDS, :].rearrange("p g n -> p (g n)"), wx_raw[:, 0:SIGMOIDS * P],
                                 ACT.Copy, scale=0.5)
            nc.scalar.activation(wx_s[:, GATE_G, :], wx_raw[:, GATE_G * P:NG * P], ACT.Copy).then_inc(wx_ready, 1)
            act.wait_ge(cond_turned, 1)
            nc.scalar.activation(hT[:, RING - 1, :], cell_ps[:, 0:N], ACT.Copy, scale=2.0).then_inc(h_ready, 1)
            nc.scalar.activation(u_of(RING - 1), cell_ps[:, 0:N], ACT.Copy, scale=2.0).then_inc(u_ready, 1)

            def body(s0, first, last):
                for j in range(BODY):
                    s, (m, c, k) = s0 + j, place(j)
                    layer0(s, j)
                    if not (first and m == 0):
                        layer1(s - LAG, (j - LAG) % RING)
                    if k == 1 and not (last and m == BODY // GS - 1):
                        copy_xT((c + 1) % 2, s - 1 + 2 * GS)
                    if k == 3 and not (first and m < 2):
                        before = 2 * s0 + 16 * (m // 2 - 1)
                        copy_out(c, s - 3 - GS, None if first else before)

            schedule(act, body)
            for k in range(GS):
                layer1(T - LAG + k, GS + k)
            for g in range(GROUPS, GROUPS + 2):
                copy_out(g % 2, GS * (g - 1), 16 * (g // 2 - 1))

        @block.vector
        def _(dve):
            def layer0_products(s, j):
                b = j % 2
                dve.wait_ge(ifg_ready, s + 1)
                nc.vector.scalar_tensor_tensor(out=pair[:, :], in0=acts[:, b, N:3 * N], scalar=1.0,
                                               in1=acts[:, b, 3 * N:5 * N], op0=ALU.add,
                                               op1=ALU.mult).then_inc(pair_ready, 1)

            def layer0_cell(s, j):
                dve.wait_ge(pair_ready, s + 1)
                for cell in (cell_ps[:, j % 2 * N:(j % 2 + 1) * N], acts[:, (j + 1) % 2, NG * N:(NG + 1) * N]):
                    nc.vector.scalar_tensor_tensor(out=cell, in0=pair[:, N:2 * N], scalar=0.5,
                                                   in1=pair[:, 0:N], op0=ALU.mult,
                                                   op1=ALU.add).then_inc(cell_ready, 1)

            def layer0_state(s, j):
                dve.wait_ge(tanh_c_ready, s + 1)
                nc.vector.scalar_tensor_tensor(out=hT[:, j % RING, :], in0=acts[:, j % 2, 0:N], scalar=1.0,
                                               in1=tanh_c[:, j % 2, :], op0=ALU.add,
                                               op1=ALU.mult).then_inc(h_ready, 1)

            def split_h(s, j):
                dve.wait_ge(h_ready, s + 2)
                nc.vector.tensor_tensor(h_rest[:, j % 2, :], hT[:, j % RING, :], upper(hT[:, j % RING, :]),
                                        ALU.subtract).then_inc(h_rest_ready, 1)
                dve.wait_ge(h_rest_ready, s + 2)
                nc.vector.tensor_tensor(h_low[:, j % 2, :], h_rest[:, j % 2, :], upper(h_rest[:, j % 2, :]),
                                        ALU.subtract).then_inc(h_low_ready, 1)

            def layer1(r, j):
                b = j % RING
                dve.wait_ge(acts1_ready, r + 1)
                nc.vector.scalar_tensor_tensor(out=pair1[:, :, :], in0=acts1[:, b, 0:2, :], scalar=1.0,
                                               in1=acts1[:, b, 2:4, :], op0=ALU.add,
                                               op1=ALU.mult).then_inc(pair1_ready, 1)
                dve.wait_ge(pair1_ready, r + 1)
                nc.vector.scalar_tensor_tensor(out=u_of(j), in0=pair1[:, 0, :], scalar=0.5,
                                               in1=pair1[:, 1, :], op0=ALU.mult,
                                               op1=ALU.add).then_inc(u_ready, 1)
                split_u_high(r, j)

            def split_u_high(r, j):
                dve.wait_ge(u_ready, r + 2)
                nc.vector.tensor_tensor(u_rest[:, j % 2, :], u_of(j), upper(u_of(j)),
                                        ALU.subtract).then_inc(u_rest_ready, 1)

            def split_u_low(r, j):
                dve.wait_ge(u_rest_ready, r + 2)
                nc.vector.tensor_tensor(u_low[:, j % 2, :], u_rest[:, j % 2, :], upper(u_rest[:, j % 2, :]),
                                        ALU.subtract).then_inc(u_low_ready, 1)

            def add_layer0(c, t0, t1):
                return nc.vector.scalar_tensor_tensor(
                    out=x1T[:, c, t0:t1, :].rearrange("p t n -> p (t n)"),
                    in0=hT[:, c * GS + t0:c * GS + t1, :].rearrange("p t n -> p (t n)"), scalar=0.5,
                    in1=xT[:, c, t0:t1, :].rearrange("p t n -> p (t n)"), op0=ALU.mult, op1=ALU.add)

            def add_layer1(c, count):
                dve.wait_ge(u_ready, count + 1)
                runs = [(0, GS)] if c == 0 else [(0, GS - 1), (GS - 1, GS)]
                for t0, t1 in runs:
                    j = c * GS + t0 + 1
                    ins = nc.vector.scalar_tensor_tensor(
                        out=sumT[:, t0:t1, :], in0=acts1[:, j % RING:j % RING + t1 - t0, 2, :], scalar=0.5,
                        in1=x1T[:, c, t0:t1, :], op0=ALU.mult, op1=ALU.add)
                ins.then_inc(sum_ready, GS)

            def split_weights(stage, parts, rest, raw, runs, done):
                if done:
                    dve.wait_ge(weights_split, done)
                if stage == 0:
                    for a, b, factor in runs:
                        ins = nc.vector.tensor_scalar(parts[:, 0, a:b], raw[:, a:b], factor, None, ALU.mult)
                elif stage == 1:
                    for a, b, factor in runs:
                        ins = nc.vector.scalar_tensor_tensor(out=rest[:, a:b], in0=raw[:, a:b], scalar=factor,
                                                             in1=parts[:, 0, a:b], op0=ALU.mult,
                                                             op1=ALU.subtract)
                elif stage == 2:
                    ins = nc.vector.tensor_copy(parts[:, 1, :], rest[:, :])
                else:
                    ins = nc.vector.tensor_tensor(parts[:, 2, :], rest[:, :], parts[:, 1, :], ALU.subtract)
                ins.then_inc(weights_split, 1)

            nc.vector.memset(acts_blank[:, :], 0.0).then_inc(blank_ready, 1)
            nc.vector.memset(acts[:, 0, NG * N:(NG + 1) * N], 0.0)
            nc.vector.memset(bias_lhs[:, :], 0.0).then_inc(setup_step, 1)
            dve.wait_ge(setup_step, 1)
            nc.vector.memset(bias_lhs[ONE_ROW:P, :], 1.0)
            dve.wait_ge(ident_ready, 1)
            nc.vector.tensor_tensor(pick_sum[:, :], ident[:, 0:NG + 2], ident[:, QUADRANT:QUADRANT + NG + 2],
                                    ALU.add).then_inc(setup_step, 1)
            dve.wait_ge(setup_step, 2)
            nc.vector.tensor_tensor(pick_sum[:, :], pick_sum[:, :],
                                    ident[:, 2 * QUADRANT:2 * QUADRANT + NG + 2], ALU.add).then_inc(setup_step, 1)
            dve.wait_ge(setup_step, 3)
            nc.vector.tensor_tensor(pick_sum[:, NG:NG + 1], pick_sum[:, NG:NG + 1],
                                    ident[:, ONE_ROW:ONE_ROW + 1], ALU.add).then_inc(setup_step, 1)
            dve.wait_ge(setup_step, 4)
            nc.vector.tensor_scalar(pick[:, 0:1], pick_sum[:, GATE_O:GATE_O + 1], 0.5, None, ALU.mult)
            nc.vector.tensor_scalar(pick[:, 1:3], pick_sum[:, GATE_I:GATE_F + 1], 0.5, None, ALU.mult)
            nc.vector.tensor_copy(pick[:, 3:4], pick_sum[:, GATE_G:GATE_G + 1])
            nc.vector.tensor_scalar(pick[:, 4:5], pick_sum[:, 4:5], 0.5, None, ALU.mult)
            nc.vector.tensor_copy(pick[:, 5:6], pick_sum[:, 5:6]).then_inc(pick_ready, 1)
            dve.wait_ge(b_in, 16 * 2)
            nc.vector.tensor_tensor(bias_rest[:, :], bias_rows[:, :], upper(bias_rows[:, :]),
                                    ALU.subtract).then_inc(setup_step, 1)
            dve.wait_ge(setup_step, 5)
            nc.vector.tensor_tensor(bias_lhs[0:NG + 2, :], bias_rest[:, :], upper(bias_rest[:, :]), ALU.subtract)
            nc.vector.tensor_copy(bias_lhs[QUADRANT:QUADRANT + NG + 2, :], upper(bias_rest[:, :]))
            nc.vector.tensor_copy(bias_lhs[2 * QUADRANT:2 * QUADRANT + NG + 2, :],
                                  upper(bias_rows[:, :])).then_inc(bias_ready, 1)
            dve.wait_ge(wh_in, 16)
            for stage in range(SPLIT_STAGES):
                split_weights(stage, wh_part, wh_rest, wh_raw,
                              ((0, SIGMOIDS * P, 0.25), (SIGMOIDS * P, NG * P, 0.5)), stage)

            def layer1_weights(stage):
                if stage == 0:
                    dve.wait_ge(w1_in, 16)
                    nc.vector.tensor_scalar(w1x_s[:, 0, :], w1_raw[:, 0, 0:P], 0.5, None, ALU.mult)
                    nc.vector.tensor_copy(w1x_s[:, 1, :], w1_raw[:, 0, P:2 * P])
                split_weights(stage, w1h_part, w1h_rest, w1_raw[:, 1, :], ((0, P, 0.25), (P, 2 * P, 0.5)),
                              SPLIT_STAGES + stage)

            def until_cell(s, j, first):
                layer0_products(s, j)
                if not (first and j <= GS):
                    split_u_low(s - LAG - 1, (j - LAG - 1) % RING)
                layer0_cell(s, j)

            def from_cell(s, j, first, final=False):
                m, c, k = place(j)
                if k == 0 and not (first and m < 2):
                    add_layer1(c, s - GS)
                if k == 3:
                    dve.wait_ge(xT_ready, s + 1)
                    dve.wait_ge(h_ready, s + 1)
                    early = add_layer0(c, 0, GS - 1)
                    if final:
                        early.then_inc(x1_early, 1)
                layer0_state(s, j)
                split_h(s, j)
                if k == 3:
                    add_layer0(c, GS - 1, GS).then_inc(x1_ready, GS)
                if first and m == 0:
                    layer1_weights(k)
                else:
                    layer1(s - LAG, (j - LAG) % RING)

            cut = BODY - 2
            for j in range(cut + 1):
                until_cell(j, j, True)
                if j < cut:
                    from_cell(j, j, True)
            with dve.Fori(BODY, T - BODY, BODY) as s0:
                from_cell(s0 - 2, cut, False)
                until_cell(s0 - 1, BODY - 1, False)
                from_cell(s0 - 1, BODY - 1, False)
                for j in range(cut + 1):
                    until_cell(s0 + j, j, False)
                    if j < cut:
                        from_cell(s0 + j, j, False)
            from_cell(T - BODY - 2, cut, False)
            until_cell(T - BODY - 1, BODY - 1, False)
            from_cell(T - BODY - 1, BODY - 1, False)
            for j in range(BODY):
                until_cell(T - BODY + j, j, False)
                from_cell(T - BODY + j, j, False, final=(j == BODY - 1))
            for k in range(GS):
                split_u_low(T - LAG + k - 1, GS + k - 1)
                if k == 0:
                    add_layer1(0, T - GS)
                layer1(T - LAG + k, GS + k)
            dve.wait_ge(out_turned, T - GS)
            add_layer1(1, T)


_INS = ["x", "cond_1024", "L0_cond_Wx", "L0_cond_Wh", "L0_cond_b", "L1_cond_weight", "L1_cond_bias"]


def kernel(**inputs):
    import numpy as _np
    import concourse.bacc as _bacc
    from concourse import mybir as _mybir
    from concourse.bass_utils import run_bass_kernel_spmd as _run

    nc = _bacc.Bacc("TRN2", target_bir_lowering=False, num_devices=1)
    arrays, args = {}, []
    for name in _INS:
        a = _np.ascontiguousarray(inputs[name])
        arrays[f"in_{name}_dram"] = a
        args.append(nc.dram_tensor(f"in_{name}_dram", a.shape, _mybir.dt.from_np(a.dtype), kind="ExternalInput").ap())
    shape = inputs["x"].shape
    out = nc.dram_tensor("out_0_dram", shape, F32, kind="ExternalOutput").ap()
    two_layer_recurrence(nc, *args, out)
    r = _run(nc, [arrays], core_ids=[0])
    return r.results[0]["out_0_dram"]
```
